# Optimizing a Trainium2 kernel written in Bass

```python
import numpy as np
import jax
import jax.numpy as jnp

def _softmax(x, axis=-1):
    return jax.nn.softmax(x, axis=axis)

def _gelu(x):
    return jax.nn.gelu(x, approximate=True)

def _silu(x):
    return jax.nn.silu(x)

def _sigmoid(x):
    return jax.nn.sigmoid(x)

def _layernorm(x, axis=-1, eps=1e-05):
    m = jnp.mean(x, axis=axis, keepdims=True)
    v = jnp.var(x, axis=axis, keepdims=True)
    return (x - m) / jnp.sqrt(v + eps)

def _scatter_add(tgt, idx, src, axis=0):
    return tgt.at[idx].add(src)

def _segment_sum(src, seg, n):
    return jax.ops.segment_sum(src, seg, n)
kernel_name = 'mk_prb_d1_jaxref_r8_7db5b9'

def setup_inputs(seed: int=0):
    np.random.seed(seed)
    _w = jnp.asarray

    def _L0_attn_setup():
        import jax, jax.numpy as jnp
        import numpy as np
        HIDDEN = 256
        HEADS = 16
        HEAD_DIM = HIDDEN // HEADS
        KV_DIM = 128
        SLOPE = 0.0625

        def alibi_bias(seq_len):
            i = jnp.arange(seq_len)[:, None]
            j = jnp.arange(seq_len)[None, :]
            return jnp.where(j <= i, -SLOPE * (i - j).astype(jnp.float32), -jnp.inf)
        key = jax.random.key(seed)
        ks = jax.random.split(key, 6)
        B, S = (2, 256)
        s = 0.02
        return {'hidden_states': jax.random.normal(ks[0], (B, S, HIDDEN), jnp.float32), 'w_dkv': jax.random.normal(ks[1], (KV_DIM, HIDDEN), jnp.float32) * s, 'w_q': jax.random.normal(ks[2], (HIDDEN, HIDDEN), jnp.float32) * s, 'w_uk': jax.random.normal(ks[3], (HIDDEN, KV_DIM), jnp.float32) * s, 'w_uv': jax.random.normal(ks[4], (HIDDEN, KV_DIM), jnp.float32) * s, 'w_o': jax.random.normal(ks[5], (HIDDEN, HIDDEN), jnp.float32) * s}
    _L0_attn_in = _L0_attn_setup()

    def _L0_ffn_setup():
        import jax, jax.numpy as jnp
        import numpy as np
        B, S, H = (4, 128, 256)
        E, K, I, SI = (16, 4, 176, 704)

        def _silu_mul(gu, inter):
            return jax.nn.silu(gu[:, :inter]) * gu[:, inter:]
        key = jax.random.key(seed)
        ks = jax.random.split(key, 7)
        s = 0.02
        return {'hidden_states': jax.random.normal(ks[0], (B, S, H), jnp.float32), 'gate_w': jax.random.normal(ks[1], (E, H), jnp.float32) * s, 'expert_gate_up': jax.random.normal(ks[2], (E, 2 * I, H), jnp.float32) * s, 'expert_down': jax.random.normal(ks[3], (E, H, I), jnp.float32) * s, 'shared_gate_up': jax.random.normal(ks[4], (2 * SI, H), jnp.float32) * s, 'shared_down': jax.random.normal(ks[5], (H, SI), jnp.float32) * s, 'shared_gate_vec': jax.random.normal(ks[6], (1, H), jnp.float32) * s}
    _L0_ffn_in = _L0_ffn_setup()
    _d = {'L0_attn_hidden_states': _L0_attn_in['hidden_states'], 'L0_attn_w_dkv': _L0_attn_in['w_dkv'], 'L0_attn_w_q': _L0_attn_in['w_q'], 'L0_attn_w_uk': _L0_attn_in['w_uk'], 'L0_attn_w_uv': _L0_attn_in['w_uv'], 'L0_attn_w_o': _L0_attn_in['w_o'], 'L0_ffn_gate_w': _L0_ffn_in['gate_w'], 'L0_ffn_expert_gate_up': _L0_ffn_in['expert_gate_up'], 'L0_ffn_expert_down': _L0_ffn_in['expert_down'], 'L0_ffn_shared_gate_up': _L0_ffn_in['shared_gate_up'], 'L0_ffn_shared_down': _L0_ffn_in['shared_down'], 'L0_ffn_shared_gate_vec': _L0_ffn_in['shared_gate_vec']}
    _x0 = _d['L0_attn_hidden_states']
    _d['L0_attn_hidden_states'] = jax.random.normal(jax.random.fold_in(jax.random.key(seed), 1), (16, 256, 256), dtype=_x0.dtype)
    del _x0
    return _d

def reference(L0_attn_hidden_states, L0_attn_w_dkv, L0_attn_w_q, L0_attn_w_uk, L0_attn_w_uv, L0_attn_w_o, L0_ffn_gate_w, L0_ffn_expert_gate_up, L0_ffn_expert_down, L0_ffn_shared_gate_up, L0_ffn_shared_down, L0_ffn_shared_gate_vec):

    def _L0_attn_ref(hidden_states, w_dkv, w_q, w_uk, w_uv, w_o):
        import jax, jax.numpy as jnp
        import numpy as np
        HIDDEN = 256
        HEADS = 16
        HEAD_DIM = HIDDEN // HEADS
        KV_DIM = 128
        SLOPE = 0.0625

        def alibi_bias(seq_len):
            i = jnp.arange(seq_len)[:, None]
            j = jnp.arange(seq_len)[None, :]
            return jnp.where(j <= i, -SLOPE * (i - j).astype(jnp.float32), -jnp.inf)
        B, S, _ = hidden_states.shape
        scale = HEAD_DIM ** (-0.5)
        c_kv = hidden_states @ w_dkv.T
        q = (hidden_states @ w_q.T).reshape(B, S, HEADS, HEAD_DIM)
        k = (c_kv @ w_uk.T).reshape(B, S, HEADS, HEAD_DIM)
        v = (c_kv @ w_uv.T).reshape(B, S, HEADS, HEAD_DIM)
        scores = jnp.einsum('bqhd,bkhd->bhqk', q, k) * scale
        scores = scores + alibi_bias(S)[None, None]
        attn = jax.nn.softmax(scores, axis=-1)
        out = jnp.einsum('bhqk,bkhd->bqhd', attn, v).reshape(B, S, HIDDEN)
        return out @ w_o.T

    def _L0_ffn_ref(hidden_states, gate_w, expert_gate_up, expert_down, shared_gate_up, shared_down, shared_gate_vec):
        import jax, jax.numpy as jnp
        import numpy as np
        B, S, H = (4, 128, 256)
        E, K, I, SI = (16, 4, 176, 704)

        def _silu_mul(gu, inter):
            return jax.nn.silu(gu[:, :inter]) * gu[:, inter:]
        orig_shape = hidden_states.shape
        x = hidden_states.reshape(-1, H)
        router_logits = x @ gate_w.T
        routing_probs = jax.nn.softmax(router_logits.astype(jnp.float32), axis=-1)
        topk_w, topk_idx = jax.lax.top_k(routing_probs, K)
        topk_w = topk_w / topk_w.sum(axis=-1, keepdims=True)
        topk_w = topk_w.astype(x.dtype)
        combine = (jax.nn.one_hot(topk_idx, E, dtype=x.dtype) * topk_w[..., None]).sum(1)
        shared = _silu_mul(x @ shared_gate_up.T, SI) @ shared_down.T
        shared = shared * jax.nn.sigmoid(x @ shared_gate_vec.T)

        def step(acc, ew):
            w_gu, w_d, cw = ew
            h = _silu_mul(x @ w_gu.T, I)
            return (acc + h @ w_d.T * cw[:, None], None)
        acc0 = jnp.zeros_like(x)
        sparse, _ = jax.lax.scan(step, acc0, (expert_gate_up, expert_down, combine.T))
        return (shared + sparse).reshape(orig_shape)
    x = L0_attn_hidden_states
    xn = _layernorm(x, axis=-1)
    x = x + _L0_attn_ref(xn, L0_attn_w_dkv, L0_attn_w_q, L0_attn_w_uk, L0_attn_w_uv, L0_attn_w_o) + _L0_ffn_ref(xn, L0_ffn_gate_w, L0_ffn_expert_gate_up, L0_ffn_expert_down, L0_ffn_shared_gate_up, L0_ffn_shared_down, L0_ffn_shared_gate_vec)
    return x

_drawn_inputs = setup_inputs


def setup_inputs(seed=0):
    import zlib

    import numpy as np

    out = dict(_drawn_inputs(seed))
    spreads = {}
    factors = {'L0_attn_w_dkv': 8.0,
     'L0_attn_w_q': 8.0,
     'L0_attn_w_uk': 8.0,
     'L0_attn_w_uv': 8.0,
     'L0_attn_w_o': 8.0,
     'L0_ffn_gate_w': 8.0,
     'L0_ffn_expert_gate_up': 7.942,
     'L0_ffn_expert_down': 7.922,
     'L0_ffn_shared_gate_up': 3.994,
     'L0_ffn_shared_down': 3.982,
     'L0_ffn_shared_gate_vec': 8.0}
    for name, (base, spread) in spreads.items():
        noise = np.random.default_rng([zlib.crc32(name.encode()), seed]).standard_normal(out[name].shape)
        drawn = base * np.exp(spread * noise) if base else spread * noise
        out[name] = jnp.asarray(drawn.astype(out[name].dtype))
    for name, factor in factors.items():
        out[name] = (out[name] * factor).astype(out[name].dtype)
    return out
```

```python
from contextlib import ExitStack

import numpy as np

import concourse.bass as bass
from concourse import mybir

F32 = mybir.dt.float32
F16 = mybir.dt.float16
BF16 = mybir.dt.bfloat16
U32 = mybir.dt.uint32
I32 = mybir.dt.int32
ALU = mybir.AluOpType
ACT = mybir.ActivationFunctionType
AX_X = mybir.AxisListType.X

P = 128
B, S, H = 16, 256, 256
TOK = B * S
HEADS, HD, KV = 16, 16, 128
E, TOPK, I, SI = 16, 4, 176, 704
KC = H // P
GT = 512
NG = TOK // GT
TT = GT // P
BG = GT // S
NF = -(-SI // P)
TILES = TOK // P
SLOT_TILES = (TOK * TOPK + E * (P - 1)) // P
PRE = 1
U = 4
SLOT_TILES = -(-SLOT_TILES // U) * U
NR = E + 1
EPS = 1e-5
NEWTON = 4
LN_STEPS = 4 + 3 * NEWTON

GU = 2 * I
EW = KC * GU + 2 * H
HALF = P // 2
assert P < I <= P + HALF
FW = 2 * KC * P + H
W_F = E * EW
W_Q = W_F + NF * FW
W_DKV = W_Q + KC * H
W_UKV = W_DKV + KC * KV
W_O = W_UKV + 2 * H
W_R = W_O + KC * H
RPAD = 32
W_ALL = W_R + KC * RPAD
CH = 2 * FW
SMALL = [(W_ALL - CH, CH), (W_Q, W_ALL - CH - W_Q)]
SHARED = [(c, CH) for c in range(W_F, W_Q, CH)]
assert NF % 2 == 0 and EW <= CH and len(SMALL) == 2 and E == 2 * NG

XS, WS = 16.0, 256.0
XW = XS * WS
QS = 4.0
SC = QS * QS * HD ** 0.5
PS = 1024.0
SLOPE = 0.0625
NEG = -(2.0 ** 100)

UNITS = 12
QT = S // P
BANK_S, BANK_T, BANK_O, BANK_X = (0, 1, 2), (3, 4), 5, (6, 7)
LAG_T, LAG_LO, LAG_V = 2, 3, 4


def unit(u):
    if u < 4:
        return 0, [2 * (4 * (u // 2) + j) + u % 2 for j in range(4)], 1
    u -= 4
    return 1, [2 * (2 * (u // 2) + j) + u % 2 for j in range(2)], 2


def lagged(n, s, lag):
    if isinstance(n, int) and (n * UNITS + s - lag < 0 or n * UNITS + s - lag >= B * UNITS):
        return None
    return (s - lag) % UNITS


def build(nc, x, wall, ident, mask, auxq, auxk, iota, tri, tids, jrow, out):
    x_v = x.rearrange("(g t p) h -> g p t h", p=P, t=TT)
    xb_v = x.rearrange("(n t p) h -> n p t h", p=P, t=QT)
    out_v = out.rearrange("(g t p) h -> g p t h", p=P, t=TT)
    xn_d = nc.dram_tensor("xn_d", (TOK, H), F32, kind="Internal").ap()
    xn_v = xn_d.rearrange("(g t p) h -> g p t h", p=P, t=TT)
    base_d = nc.dram_tensor("base_d", (B, P, QT * H), F32, kind="Internal").ap()
    ids_d = nc.dram_tensor("ids_d", (P * SLOT_TILES, 1), I32, kind="Internal").ap()
    y_d = nc.dram_tensor("y_d", (SLOT_TILES * P, H), F32, kind="Internal").ap()

    with ExitStack() as ctx:
        def sb(name, shape, dt=F32):
            return ctx.enter_context(nc.sbuf_tensor(name, shape, dt))

        def sem(name):
            return ctx.enter_context(nc.semaphore(name))

        bank = [ctx.enter_context(nc.psum_tensor(f"bank{i}", [P, 512], F32)) for i in range(8)]
        bank16 = [b[:, :].bitcast(F16) for b in bank]

        whi = sb("whi", [P, W_ALL], F16)
        wlo = sb("wlo", [P, W_ALL], F16)
        xhi = sb("xhi", [P, KC, TOK], F16)
        xlo = sb("xlo", [P, KC, TOK], F16)
        idf = sb("idf", [P, P])
        idh = sb("idh", [P, P], F16)
        idb = sb("idb", [P, P], BF16)
        maskb = sb("maskb", [P, P], BF16)
        trih = sb("trih", [P, P], F16)
        onesh = sb("onesh", [P, P], F16)
        aux = sb("aux", [P, 2, 2, 16])
        iot = sb("iot", [P, E])
        tid = sb("tid", [P, TILES], I32)
        cw4 = sb("cw4", [P, TILES, TOPK])
        sgate = sb("sgate", [P, TILES])
        slot = sb("slot", [P, TILES * TOPK], I32)
        place = sb("place", [P, TILES * TOPK], I32)
        ids = sb("ids", [P, SLOT_TILES], I32)
        idp = sb("idp", [P, 2, TOPK + 1], I32)
        texp = sb("texp", [1, SLOT_TILES], I32)

        arena = sb("arena", [P, 17628])

        def view(at, shape, dt=F32):
            n = int(np.prod(shape))
            n32 = n if dt in (F32, I32, U32) else n // 2
            v = arena[:, at:at + n32]
            if dt != F32:
                v = v.bitcast(dt)
            names = "abcd"[:len(shape)]
            if len(shape) > 1:
                v = v.rearrange(f"p ({' '.join(names)}) -> p {' '.join(names)}", **dict(zip(names[1:], shape[1:])))
            return v, at + n32

        xin, a = view(0, [TT, H])
        xn, a = view(a, [TT, H])
        stage0, a = view(a, [CH])
        stage1, a = view(a, [CH])
        stage = [stage0, stage1]
        stats, a = view(a, [TT, 6])
        mv, a = view(a, [TT, 2])
        var, a = view(a, [TT])
        nwt, a = view(a, [TT])
        rstd, a = view(a, [TT])
        lg, a = view(a, [TT, RPAD])
        mx8, a = view(a, [TT, 8])
        ix8, a = view(a, [TT, 8], U32)
        ixf, a = view(a, [TT, 8])
        d4, a = view(a, [TILES, TOPK])
        zs, a = view(a, [TILES, 1])
        eq, a = view(a, [TILES, E, TOPK], F16)
        msk, a = view(a, [TILES, E], F16)
        e4, a = view(a, [TILES, TOPK])
        tz, a = view(a, [TILES])
        s4, a = view(a, [TILES])
        r4, a = view(a, [TILES])
        pre, a = view(a, [2, (TILES + 1) * E], F16)
        nti, a = view(a, [E], I32)
        nth, a = view(a, [E], I32)
        scan0, a = view(a, [2 * E])
        scan1, a = view(a, [2 * E])
        slf, a = view(a, [TILES, E])
        prod, a = view(a, [TILES, E * TOPK])
        slk, a = view(a, [TILES * TOPK])
        pf, a = view(a, [TILES * TOPK])
        ti, a = view(a, [TILES * TOPK], I32)
        maskf, a = view(a, [P])
        trif, a = view(a, [P])
        xres, a = view(0, [QT, H])
        base, a = view(a, [QT, H])
        qT, a = view(a, [8, 2 * S], F16)
        kT, a = view(a, [8, 2 * S], F16)
        chi, a = view(a, [S], F16)
        clo, a = view(a, [S], F16)
        qs, a = view(a, [QT, HEADS, 64], F16)
        ks, a = view(a, [QT, HEADS, 64], F16)
        vs, a = view(a, [2 * QT, HEADS, 34], F16)
        nmax, a = view(a, [3, 4])
        nbias, a = view(a, [3, 4])
        rrec, a = view(a, [QT, HEADS])
        prob, a = view(a, [3, 4, P])
        pthi, a = view(a, [4, 4 * P], F16)
        ptlo, a = view(a, [4, 4 * P], F16)
        onat, a = view(a, [2, QT, H])
        ohi, a = view(a, [KC, S], F16)
        olo, a = view(a, [KC, S], F16)
        hx, a = view(a, [2, 2 * P])
        firsts, b = view(a, [E])
        jr, b = view(b, [SLOT_TILES])
        ge, b = view(b, [SLOT_TILES, E])
        xg, a = view(a, [U, H])
        idc, a = view(a, [U], I32)
        xgh, a = view(a, [2, KC * P], F16)
        xgl, a = view(a, [2, KC * P], F16)
        sg, a = view(a, [2, I])
        hth, a = view(a, [2, 2 * P], F16)
        htl, a = view(a, [2, 2 * P], F16)
        yb, a = view(a, [U, H])
        baser, a = view(0, [TT, H])
        yout, a = view(a, [TT, H])
        yg, a = view(a, [TT, TOPK, H])
        idy, a = view(a, [TT, TOPK], I32)
        sgs, a = view(a, [2, GT])
        hf, a = view(a, [2, GT])
        hhi, a = view(a, [2, GT], F16)
        hlo, a = view(a, [2, GT], F16)
        acc, a = view(a, [TT, 2, H])

        const_in = sem("const_in")
        w_in = [sem(f"w_in{i}") for i in range(2)]
        whi_done = sem("whi_done")
        small_done = sem("small_done")
        pair_done = sem("pair_done")
        wlo_done = sem("wlo_done")
        prep = sem("prep")
        zero_done = sem("zero_done")
        x_in = sem("x_in")
        xs_done = sem("xs_done")
        ln_stat = sem("ln_stat")
        stat_done = sem("stat_done")
        xn_done = sem("xn_done")
        xt_ps = sem("xt_ps")
        xhi_done = sem("xhi_done")
        xlo_done = sem("xlo_done")
        rt_ps = sem("rt_ps")
        lg_done = sem("lg_done")
        rt_step = sem("rt_step")
        top_done = sem("top_done")
        e4_done = sem("e4_done")
        pl_step = sem("pl_step")
        pre_done = sem("pre_done")
        te_step = sem("te_step")
        pos_ps = sem("pos_ps")
        place_done = sem("place_done")
        copy_done = [sem(f"copy_done{i}") for i in range(2)]
        idc_done = sem("idc_done")
        idy_done = sem("idy_done")
        scat = [sem(f"scat{i}") for i in range(2)]
        ids_in = sem("ids_in")

        aux_done = sem("aux_done")
        xres_in = sem("xres_in")
        c_ps = sem("c_ps")
        chi_done = sem("chi_done")
        clo_done = sem("clo_done")
        q_ps = sem("q_ps")
        qhi_done = sem("qhi_done")
        qlo_done = sem("qlo_done")
        kv_ps = sem("kv_ps")
        kvhi_done = sem("kvhi_done")
        kvlo_done = sem("kvlo_done")
        qT_ps = sem("qT_ps")
        kT_ps = sem("kT_ps")
        qT_done = sem("qT_done")
        kT_done = sem("kT_done")
        s_ps = sem("s_ps")
        max_done = sem("max_done")
        bias_done = sem("bias_done")
        exp_done = sem("exp_done")
        pt_ps = sem("pt_ps")
        pthi_done = sem("pthi_done")
        ptlo_done = sem("ptlo_done")
        pv_ps = sem("pv_ps")
        rrec_done = sem("rrec_done")
        o_used = sem("o_used")
        oT_ps = sem("oT_ps")
        ohi_done = sem("ohi_done")
        olo_done = sem("olo_done")
        wo_ps = sem("wo_ps")
        base_done = sem("base_done")
        bs_done = sem("bs_done")

        xg_in = [sem(f"xg_in{i}") for i in range(U)]
        tx_ps = sem("tx_ps")
        xgh_done = sem("xgh_done")
        xgl_done = sem("xgl_done")
        gu_ps = sem("gu_ps")
        sg_done = sem("sg_done")
        h_done = sem("h_done")
        th_ps = sem("th_ps")
        hth_done = sem("hth_done")
        htl_done = sem("htl_done")
        y_ps = sem("y_ps")
        y_done = [sem(f"y_done{i}") for i in range(2)]
        ys_done = [sem(f"ys_done{i}") for i in range(U)]

        base_in = sem("base_in")
        g_ps = sem("g_ps")
        u_ps = sem("u_ps")
        silu_done = sem("silu_done")
        f_done = sem("f_done")
        fhi_done = sem("fhi_done")
        flo_done = sem("flo_done")
        d_ps = sem("d_ps")
        yg_in = [sem(f"yg_in{i}") for i in range(TT)]
        d_used = sem("d_used")
        acc_done = sem("acc_done")
        tok_done = sem("tok_done")
        out_done = sem("out_done")

        block = ctx.enter_context(nc.Block())

        def cols(off, n, m):
            return whi[:, off + n * m:off + (n + 1) * m], wlo[:, off + n * m:off + (n + 1) * m]

        def link(eng, sem_, base_, ins, n):
            ins.then_inc(sem_, 1)
            eng.wait_ge(sem_, base_ + n)

        def attention(eng, step, extra, drain):
            def batch(n, half):
                for s in range(UNITS):
                    step(n, s, half, extra)

            for s in range(UNITS):
                extra(-1, s, 1)
            batch(0, 0)
            with eng.Fori(0, (B - 2) // 2) as i:
                batch(2 * i + 1, 1)
                batch(2 * i + 2, 0)
            batch(B - 1, 1)
            for s in range(drain):
                step(B, s, 0, lambda n, s, half: None)
            for s in range(UNITS):
                extra(B, s, 0)

        def expert_rounds(eng, steps):
            last = SLOT_TILES // U

            def take(i, u, k):
                n = i * U + u - k
                r = i if u >= k else i - 1
                if steps[k] is None or (isinstance(i, int) and not 0 <= n < SLOT_TILES):
                    return
                steps[k](*((n, (u - k) % U, r) if k == 3 else (n, (u - k) % U)))

            for u in range(U):
                for k in range(4):
                    take(0, u, k)
            with eng.Fori(1, last) as i:
                for u in range(U):
                    for k in range(4):
                        take(i, u, k)
            for u in range(3):
                for k in range(4):
                    take(last, u, k)

        @block.sync
        def _(sp):
            for s, n in ((xs_done, 16), (wlo_done, 2), (o_used, 1), (bs_done, 16),
                         (tx_ps, U), (xgl_done, 2), (h_done, 2), (htl_done, 2), (y_done[0], 1), (y_done[1], 1),
                         *((s, 16) for s in ys_done), (f_done, 2), (d_used, 4), (tok_done, 4), (out_done, 16)):
                sp.sem_inc(s, n)
            sp.dma_start(xin, x_v[0]).then_inc(x_in, 16)
            for dst, src in ((idf[:, :], ident), (maskf[:, :], mask), (iot[:, :], iota), (trif[:, :], tri),
                             (aux[:, 0], auxq), (aux[:, 1], auxk), (tid[:, :], tids), (jr[0:1, :], jrow)):
                sp.dma_start(dst, src).then_inc(const_in, 16)
            for n, (c, m) in enumerate(SMALL):
                sp.dma_start(stage[n][:, 0:m], wall[:, c:c + m]).then_inc(w_in[n], 16)

            sp.wait_ge(small_done, 2)

            def expert_weights(g):
                for u in range(2):
                    sp.wait_ge(wlo_done, 2 * g + u + 1)
                    sp.dma_start(stage[u][:, 0:EW], wall[:, bass.ds((2 * g + u) * EW, EW)]).then_inc(w_in[u], 16)

            with sp.Fori(0, NG - 1) as g:
                expert_weights(g)
                sp.wait_ge(xn_done, g * TT + TT)
                sp.dma_start(xin, x_v[g + 1]).then_inc(x_in, 16)
                sp.dma_start(xn_v[g], xn).then_inc(xs_done, 16)
            expert_weights(NG - 1)
            sp.wait_ge(xn_done, NG * TT)
            sp.dma_start(xn_v[NG - 1], xn).then_inc(xs_done, 16)
            for n, (c, m) in enumerate(SHARED):
                sp.wait_ge(wlo_done, n + 1 + E)
                sp.dma_start(stage[n % 2][:, 0:m], wall[:, c:c + m]).then_inc(w_in[n % 2], 16)
            sp.wait_ge(zero_done, 1)
            sp.dma_start(ids_d.rearrange("(p j) a -> p (j a)", p=P), ids[:, :]).then_inc(zero_done, 16)

            sp.wait_ge(xs_done, 16 * NG + 16)
            sp.wait_ge(place_done, 2)
            sp.dma_start(xres, xb_v[0]).then_inc(xres_in, 16)
            with sp.Fori(0, B - 1) as n:
                sp.wait_ge(base_done, n + 1)
                sp.dma_start(base_d[n].rearrange("p (t h) -> p t h", t=QT), base).then_inc(bs_done, 16)
                sp.dma_start(xres, xb_v[n + 1]).then_inc(xres_in, 16)
            sp.wait_ge(base_done, B)
            sp.dma_start(base_d[B - 1].rearrange("p (t h) -> p t h", t=QT), base).then_inc(bs_done, 16)
            sp.wait_ge(bs_done, 16 * B + 16)
            base_v = base_d.rearrange("(g b) p h -> g p b h", b=BG)
            baser_v = baser.rearrange("p (b t) h -> p b (t h)", b=BG)
            sp.dma_start(baser_v, base_v[0]).then_inc(base_in, 16)

            with sp.Fori(0, SLOT_TILES // U) as i:
                for u in range(U):
                    sp.wait_ge(y_done[u % 2], i * (U // 2) + u // 2 + 2)
                    sp.dma_start(y_d.rearrange("(j p) h -> j p h", p=P)[i * U + u], yb[:, u]).then_inc(ys_done[u], 16)

            with sp.Fori(0, NG - 1) as g:
                sp.wait_ge(d_used, g * TT + 8)
                sp.dma_start(baser_v, base_v[g + 1]).then_inc(base_in, 16)
                sp.wait_ge(tok_done, g * TT + 8)
                sp.dma_start(out_v[g], yout).then_inc(out_done, 16)
            sp.wait_ge(tok_done, NG * TT + 4)
            sp.dma_start(out_v[NG - 1], yout).then_inc(out_done, 16)
            sp.wait_ge(out_done, 16 * NG + 16)

        @block.gpsimd
        def _(pool):
            nc.gpsimd.memset(ids[:, :], 0).then_inc(zero_done, 1)

            def weights_lo(count, u, c, m):
                pool.wait_ge(whi_done, count)
                nc.gpsimd.tensor_tensor(wlo[:, c], stage[u][:, 0:m], whi[:, c], ALU.subtract).then_inc(wlo_done, 1)

            with pool.Fori(0, NG) as g:
                for u in range(2):
                    weights_lo(2 * g + u + 3, u, bass.ds((2 * g + u) * EW, EW), EW)
                    pool.wait_ge(wlo_done, 2 * g + u + 3)
                    c = bass.ds((2 * g + u) * EW + EW - H, H)
                    nc.gpsimd.tensor_copy(whi[HALF:, c], wlo[HALF:, c]).then_inc(pair_done, 1)
                    pool.wait_ge(pair_done, 2 * g + u + 1)
            for n, (c, m) in enumerate(SHARED):
                weights_lo(n + 3 + E, n % 2, slice(c, c + m), m)
            pool.wait_ge(place_done, 2)
            pool.wait_ge(zero_done, 17)
            def scatter(i):
                for u in range(2):
                    t = 2 * i + (u - 2)
                    if not isinstance(i, int):
                        pool.wait_ge(scat[u], i * 64 - 64)
                    nc.gpsimd.tensor_copy(idp[:, u, 0:TOPK], place[:, bass.ds(t * TOPK, TOPK)])
                    nc.gpsimd.tensor_copy(idp[:, u, TOPK:TOPK + 1], tid[:, bass.ds(t, 1)]).then_inc(copy_done[u], 1)
                    pool.wait_ge(zero_done, 17)
                    pool.wait_ge(copy_done[u], i)
                    for k in range(TOPK):
                        nc.gpsimd.indirect_dma_start(ids_d, bass.IndirectOffsetOnAxis(idp[:, u, k:k + 1], 0),
                                                     idp[:, u, TOPK:TOPK + 1], None).then_inc(scat[u], 16)

            scatter(1)
            with pool.Fori(2, TILES // 2 + 1) as i:
                scatter(i)
            width = E
            while width > 1:
                width //= 2
                pool.wait_ge(te_step, E.bit_length() - width.bit_length())
                nc.gpsimd.tensor_tensor(ge[0:1, :, 0:width], ge[0:1, :, 0:width], ge[0:1, :, width:2 * width],
                                        ALU.add).then_inc(te_step, 1)
            pool.wait_ge(te_step, E.bit_length())
            nc.gpsimd.tensor_scalar(texp[:, :], ge[0:1, :, 0], float(EW), float(-EW), ALU.mult, ALU.add).then_inc(te_step, 1)
            pool.wait_ge(te_step, E.bit_length() + 1)
            for i in range(2):
                pool.wait_ge(scat[i], 64 * TILES // 2)
            nc.gpsimd.dma_start(ids[:, :], ids_d.rearrange("(p j) a -> p (j a)", p=P)).then_inc(ids_in, 16)
            pool.wait_ge(ids_in, 16)
            pool.wait_ge(xs_done, 16 * NG + 16)
            with pool.Fori(0, SLOT_TILES // U) as i:
                for u in range(U):
                    pool.wait_ge(tx_ps, i * U + u + 1)
                    nc.gpsimd.tensor_copy(idc[:, u:u + 1], ids[:, bass.ds(i * U + u, 1)]).then_inc(idc_done, 1)
                    pool.wait_ge(zero_done, 17)
                    pool.wait_ge(idc_done, i * U + u + 1)
                    nc.gpsimd.indirect_dma_start(xg[:, u], None, xn_d,
                                                 bass.IndirectOffsetOnAxis(idc[:, u:u + 1], 0)).then_inc(xg_in[u], 16)
            for u in range(U):
                pool.wait_ge(ys_done[u], 16 * SLOT_TILES // U + 16)
            with pool.Fori(0, NG) as g:
                for t in range(TT):
                    pool.wait_ge(tok_done, g * TT + t + 1)
                    nc.gpsimd.tensor_copy(idy[:, t], slot[:, bass.ds((g * TT + t) * TOPK, TOPK)]).then_inc(idy_done, 1)
                    pool.wait_ge(zero_done, 17)
                    pool.wait_ge(idy_done, g * TT + t + 1)
                    for k in range(TOPK):
                        nc.gpsimd.indirect_dma_start(yg[:, t, k], None, y_d,
                                                     bass.IndirectOffsetOnAxis(idy[:, t, k:k + 1], 0)).then_inc(yg_in[t], 16)

        @block.scalar
        def _(act):
            def weights_hi(count, u, c, m):
                act.wait_ge(w_in[u], count)
                nc.scalar.activation(whi[:, c], stage[u][:, 0:m], ACT.Copy, scale=WS)
                nc.scalar.activation(stage[u][:, 0:m], stage[u][:, 0:m], ACT.Copy, scale=WS).then_inc(whi_done, 1)

            for n, (c, m) in enumerate(SMALL):
                act.wait_ge(w_in[n], 16)
                nc.scalar.activation(whi[:, c:c + m], stage[n][:, 0:m], ACT.Copy, scale=WS).then_inc(whi_done, 1)
            with act.Fori(0, NG) as g:
                for c in range(KC):
                    act.wait_ge(xt_ps, g * KC + c + 1)
                    nc.scalar.activation(xhi[:, c, bass.ds(g * GT, GT)], bank[c][:, :], ACT.Copy, scale=XS)\
                      .then_inc(xhi_done, 1)
                for u in range(2):
                    weights_hi(g * 16 + 32, u, bass.ds((2 * g + u) * EW, EW), EW)
            for n, (c, m) in enumerate(SHARED):
                if n == 1:
                    act.wait_ge(top_done, NG)
                    nc.scalar.activation(e4, d4, ACT.Exp, scale=1.0 / XW)
                    nc.scalar.activation(tz, zs[:, :, 0], ACT.Tanh, scale=0.5 / XW).then_inc(e4_done, 1)
                weights_hi(16 * (2 + NG + n // 2), n % 2, slice(c, c + m), m)
            act.wait_ge(aux_done, 1)

            def exps(n, u):
                qt, heads, nk = unit(u)
                act.wait_ge(bias_done, n * UNITS + u + 1)
                sc = bank[BANK_S[u % 3]][:, :].rearrange("p (h k) -> p h k", k=nk * P)
                pr = prob[:, u % 3].rearrange("p b k -> p (b k)").rearrange("p (h k) -> p h k", k=nk * P)
                for j in range(len(heads)):
                    last = nc.scalar.activation(pr[:, j], sc[:, j], ACT.Exp, bias=nbias[:, u % 3, j:j + 1], scale=1.0 / SC)
                last.then_inc(exp_done, 1)

            def extra(n, s, half):
                m = n + 1
                here = not isinstance(n, int) or n < B - 1
                to = 1 - half
                if s == 0 and here:
                    act.wait_ge(c_ps, m + 1)
                    nc.scalar.activation(chi, bank[BANK_X[1]][:, 0:S], ACT.Copy, scale=XS / XW).then_inc(chi_done, 1)
                if s == 1 and here:
                    act.wait_ge(q_ps, m + 1)
                    src = bank[BANK_X[0]][:, :].rearrange("p (h a d) -> p h a d", a=1, d=HD)
                    nc.scalar.activation(qs.rearrange("p t h (a d) -> p (t h) a d", a=4)[:, :, 0:3:2],
                                         src.broadcast_to([P, QT * HEADS, 2, HD]), ACT.Copy,
                                         scale=QS / XW).then_inc(qhi_done, 1)
                if s in (3, 4) and here:
                    t = s - 3
                    x_ = bank[BANK_X[1 - t]]
                    act.wait_ge(kv_ps, m * QT + t + 1)
                    src = x_[:, 0:H].rearrange("p (h a d) -> p h a d", a=1, d=HD)
                    nc.scalar.activation(ks[:, t, :, 0:2 * HD].rearrange("p h (a d) -> p h a d", a=2),
                                         src.broadcast_to([P, HEADS, 2, HD]), ACT.Copy, scale=QS / XW)
                    nc.scalar.activation(vs[:, to * QT + t, :, 0:HD], x_[:, H:2 * H].rearrange("p (h d) -> p h d", d=HD),
                                         ACT.Copy, scale=XS / XW).then_inc(kvhi_done, 1)
                if s in (7, 9) and here:
                    t = (s - 7) // 2
                    act.wait_ge(qT_ps, m * QT + t + 1)
                    nc.scalar.copy(qT[:, :, to * S + t * P:to * S + (t + 1) * P],
                                   bank16[BANK_X[1]].rearrange("p (c q) -> p c q", c=8)).then_inc(qT_done, 1)
                if s == 5 and (not isinstance(n, int) or n > 0):
                    act.wait_ge(oT_ps, n)
                    nc.scalar.activation(ohi.rearrange("p c q -> p (c q)"), bank[BANK_X[1]][:, :],
                                         ACT.Copy).then_inc(ohi_done, 1)

            def step(n, s, half, extra):
                if s:
                    extra(n, s - 1, half)
                if lagged(n, s, LAG_T) is not None:
                    act.wait_ge(pt_ps, n * UNITS + s - LAG_T + 1)
                    nc.scalar.activation(pthi[:, (s - LAG_T) % 4], bank[BANK_T[(s - LAG_T) % 2]][:, :], ACT.Copy,
                                         scale=PS).then_inc(pthi_done, 1)
                if lagged(n, s, 0) is not None:
                    exps(n, s)

            attention(act, step, extra, LAG_T)

            def rows_hi(n, u):
                act.wait_ge(tx_ps, n + 1 + U)
                nc.scalar.activation(xgh[:, u % 2], bank[u % 2][:, 0:2 * P], ACT.Copy, scale=XS).then_inc(xgh_done, 1)

            def silu(n, u):
                act.wait_ge(gu_ps, n + 1)
                nc.scalar.activation(sg[:, u % 2], bank[2 + u % 2][:, 0:I], ACT.Silu, scale=1.0 / XW).then_inc(sg_done, 1)

            def inner_hi(n, u):
                act.wait_ge(th_ps, n + 1)
                nc.scalar.activation(hth[:, u % 2], bank[4 + u % 2][:, 0:2 * P], ACT.Copy).then_inc(hth_done, 1)

            def rows_out(n, u, rounds):
                if u % 2:
                    return
                act.wait_ge(y_ps, n + 1)
                act.wait_ge(ys_done[u], rounds * 16 + 16)
                nc.scalar.activation(yb[:, u], bank[6][:, 0:H], ACT.Copy, scale=1.0 / XW).then_inc(y_done[0], 1)

            steps = (rows_hi, silu, inner_hi, rows_out)
            expert_rounds(act, steps)

            with act.Fori(0, NG) as g:
                for f in range(NF):
                    act.wait_ge(g_ps, g * NF + f + 1)
                    nc.scalar.activation(sgs[:, f % 2], bank[2 * (f % 2)][:, :], ACT.Silu, scale=1.0 / XW)\
                      .then_inc(silu_done, 1)
                    act.wait_ge(f_done, g * NF + f + 3)
                    nc.scalar.activation(hhi[:, f % 2], hf[:, f % 2], ACT.Copy).then_inc(fhi_done, 1)

        @block.vector
        def _(dve):
            V = nc.vector
            def norm(g):
                dve.wait_ge(x_in, g * 16 + 16)
                for t in range(TT):
                    last = V.bn_stats(stats[:, t], xin[:, t])
                last.then_inc(stat_done, 1)
                dve.wait_ge(stat_done, g + 1)
                V.memset(nwt, 0.0)
                for t in range(TT):
                    last = V.bn_aggr(mv[:, t], stats[:, t])
                last.then_inc(ln_stat, 1)
                dve.wait_ge(ln_stat, g * LN_STEPS + 1)
                n = 1

                def step(ins):
                    nonlocal n
                    n += 1
                    link(dve, ln_stat, g * LN_STEPS, ins, n)

                step(V.tensor_scalar(var, mv[:, :, 1], EPS, None, ALU.add))
                step(V.tensor_scalar(rstd.bitcast(I32), var.bitcast(I32), 1, None, ALU.logical_shift_right))
                step(V.tensor_scalar(rstd.bitcast(I32), rstd.bitcast(I32), -1.0, float(0x5F3759DF), ALU.mult, ALU.add))
                for _ in range(NEWTON):
                    step(V.scalar_tensor_tensor(nwt, rstd, -0.5, rstd, ALU.mult, ALU.mult))
                    step(V.tensor_tensor(nwt, nwt, var, ALU.mult))
                    step(V.scalar_tensor_tensor(rstd, nwt, 1.5, rstd, ALU.add, ALU.mult))
                assert n == LN_STEPS
                dve.wait_ge(xs_done, g * 16 + 16)
                for t in range(TT):
                    V.tensor_scalar(xn[:, t], xin[:, t], mv[:, t, 0:1], rstd[:, t:t + 1],
                                    ALU.subtract, ALU.mult).then_inc(xn_done, 1)

            STEPS = 4

            def top(g):
                dve.wait_ge(rt_ps, g + 1)
                n = 0

                def step(ins):
                    nonlocal n
                    n += 1
                    link(dve, rt_step, g * STEPS, ins, n)

                V.tensor_copy(lg[:, :, 0:NR], bank[2][:, 0:TT * RPAD].rearrange("p (t e) -> p t e", t=TT)[:, :, 0:NR])\
                 .then_inc(lg_done, 1)
                dve.wait_ge(prep, 1)
                dve.wait_ge(lg_done, g + 1)
                for t in range(TT):
                    last = V.max(mx8[:, t], lg[:, t, 0:E])
                step(last)
                V.tensor_copy(zs[:, bass.ds(g * TT, TT)], lg[:, :, E:NR])
                V.tensor_tensor(d4[:, bass.ds(g * TT, TT)], mx8[:, :, 0:TOPK], mx8[:, :, 0:1].broadcast_to([P, TT, TOPK]),
                                ALU.subtract)
                for t in range(TT):
                    last = V.max_index(ix8[:, t], mx8[:, t], lg[:, t, 0:E])
                step(last)
                step(V.tensor_copy(ixf, ix8))
                for t in range(TT):
                    last = V.tensor_tensor(eq[:, bass.ds(g * TT + t, 1)].rearrange("p a e k -> p (a e) k"),
                                           iot[:, :].rearrange("p (e a) -> p e a", a=1).broadcast_to([P, E, TOPK]),
                                           ixf[:, t:t + 1, 0:TOPK].broadcast_to([P, E, TOPK]), ALU.is_equal)
                step(last)
                with nc.allow_low_precision("zeros and ones"):
                    V.tensor_reduce(msk[:, bass.ds(g * TT, TT)], eq[:, bass.ds(g * TT, TT)], AX_X, ALU.add)\
                     .then_inc(top_done, 1)
                assert n == STEPS

            def rows_turned_lo(g):
                for c in range(KC):
                    dve.wait_ge(xhi_done, g * KC + c + 1)
                    V.scalar_tensor_tensor(xlo[:, c, bass.ds(g * GT, GT)], bank[c][:, :], XS, xhi[:, c, bass.ds(g * GT, GT)],
                                           ALU.mult, ALU.subtract).then_inc(xlo_done, 1)

            norm(0)
            dve.wait_ge(const_in, 16 * 8)
            V.tensor_copy(idh[:, :], idf[:, :])
            V.tensor_copy(idb[:, :], idf[:, :])
            V.tensor_copy(maskb[:, :], maskf[:, :])
            V.tensor_copy(trih[:, :], trif[:, :])
            V.memset(onesh[:, :], 1.0)
            V.memset(scan0, 0.0)
            V.memset(pre, 0.0)
            V.memset(scan1, 0.0).then_inc(prep, 1)

            V.memset(hx[:, :, I:2 * P], 0.0)
            for n, (c, m) in enumerate(SMALL):
                dve.wait_ge(whi_done, n + 1)
                V.scalar_tensor_tensor(wlo[:, c:c + m], stage[n][:, 0:m], WS, whi[:, c:c + m], ALU.mult, ALU.subtract)\
                 .then_inc(small_done, 1)
            with dve.Fori(0, NG - 1) as g:
                rows_turned_lo(g)
                norm(g + 1)
                top(g)
            rows_turned_lo(NG - 1)
            top(NG - 1)

            done = 0

            def step(ins):
                nonlocal done
                done += 1
                link(dve, pl_step, 0, ins, done)

            dve.wait_ge(top_done, NG)
            mskf = msk.rearrange("p t e -> p (t e)")
            src = 0
            with nc.allow_low_precision("counts up to 32"):
                step(V.tensor_copy(pre[:, 0, E:], mskf))
                for d in (1, 2, 4, 8, 16):
                    n = d * E
                    V.tensor_copy(pre[:, 1 - src, 0:n + E], pre[:, src, 0:n + E])
                    ins = V.tensor_tensor(pre[:, 1 - src, n + E:], pre[:, src, n + E:], pre[:, src, E:-n], ALU.add)
                    src = 1 - src
                    if d < TILES // 2:
                        step(ins)
                ins.then_inc(pre_done, 1)
            assert src == PRE
            dve.wait_ge(e4_done, 1)
            step(V.tensor_reduce(s4, e4, AX_X, ALU.add))
            step(V.reciprocal(r4, s4))
            V.tensor_tensor(cw4[:, :, :], e4, r4.rearrange("p (t a) -> p t a", a=1).broadcast_to([P, TILES, TOPK]), ALU.mult)
            V.tensor_scalar(sgate[:, :], tz, 1.0, 0.5 / XW, ALU.add, ALU.mult)
            dve.wait_ge(pos_ps, 1)
            step(V.tensor_scalar(nti, bank[1][:, 0:E], float(P - 1), None, ALU.add))
            step(V.tensor_scalar(nth, nti, P.bit_length() - 1, None, ALU.logical_shift_right))
            a_, b_ = scan0, scan1
            step(V.tensor_copy(a_[:, E:2 * E], nth))
            for d in (1, 2, 4, 8):
                step(V.tensor_tensor(b_[:, E:2 * E], a_[:, E:2 * E], a_[:, E - d:2 * E - d], ALU.add))
                a_, b_ = b_, a_
            first = a_[:, E - 1:2 * E - 1]
            V.tensor_copy(firsts[0:1], first[0:1])
            step(V.scalar_tensor_tensor(slf, first.rearrange("p (a e) -> p a e", a=1).broadcast_to([P, TILES, E]), float(P),
                                        bank[0][:, :].rearrange("p (t e) -> p t e", e=E), ALU.mult, ALU.add))
            step(V.tensor_tensor(prod.rearrange("p t (e k) -> p t e k", k=TOPK).rearrange("p t e k -> p (t e) k"),
                                 eq.rearrange("p t e k -> p (t e) k"),
                                 slf.rearrange("p t (e a) -> p (t e) a", a=1).broadcast_to([P, TILES * E, TOPK]), ALU.mult))
            step(V.tensor_reduce(slk.rearrange("p (t k) -> p t k", k=TOPK),
                                 prod.rearrange("p t (e k) -> p t k e", k=TOPK), AX_X, ALU.add))
            step(V.tensor_copy(slot[:, :], slk))
            step(V.tensor_scalar(ti, slot[:, :], P - 1, None, ALU.bitwise_and))
            step(V.tensor_copy(pf, ti))
            step(V.tensor_scalar(ti, slot[:, :], P.bit_length() - 1, None, ALU.logical_shift_right))
            step(V.tensor_copy(slk, ti))
            V.scalar_tensor_tensor(place[:, :], pf, float(SLOT_TILES), slk, ALU.mult, ALU.add).then_inc(place_done, 1)
            dve.wait_ge(place_done, 1)
            dve.wait_ge(xs_done, 16 * NG + 16)
            dve.wait_ge(wlo_done, 2 + E + len(SHARED))
            V.memset(vs[:, :, :, HD:HD + 1], 1.0)
            V.memset(qs[:, :, :, 48:64], 0.0)
            V.memset(ks[:, :, :, 48:64], 0.0).then_inc(place_done, 1)
            dve.wait_ge(place_done, 2)
            for t in range(QT):
                for n, buf in enumerate((qs, ks)):
                    last = V.tensor_copy(buf[:, t, :, 48:50], aux[:, n, t:t + 1, 0:2].broadcast_to([P, HEADS, 2]))
            last.then_inc(aux_done, 1)

            def tile_out(n, qt, half):
                dve.wait_ge(pv_ps, n * UNITS + (12 if qt else 4))
                o = bank[BANK_O][:, :].rearrange("p (h c) -> p h c", h=HEADS)
                V.reciprocal(rrec[:, qt].rearrange("p (h a) -> p h a", a=1), o[:, :, HD:HD + 1]).then_inc(rrec_done, 1)
                dve.wait_ge(rrec_done, n * QT + qt + 1)
                V.tensor_tensor(onat[:, half, qt].rearrange("p (h d) -> p h d", d=HD), o[:, :, 0:HD],
                                rrec[:, qt].rearrange("p (h a) -> p h a", a=1).broadcast_to([P, HEADS, HD]),
                                ALU.mult).then_inc(o_used, 1)

            def row_max(n, u):
                qt, heads, nk = unit(u)
                dve.wait_ge(s_ps, n * UNITS + u + 1)
                V.tensor_reduce(nmax[:, u % 3, 0:len(heads)],
                                bank[BANK_S[u % 3]][:, :].rearrange("p (h k) -> p h k", k=nk * P),
                                AX_X, ALU.max, negate=True).then_inc(max_done, 1)

            def bias(n, u):
                heads = unit(u)[1]
                dve.wait_ge(max_done, n * UNITS + u + 1)
                V.tensor_scalar(nbias[:, u % 3, 0:len(heads)], nmax[:, u % 3, 0:len(heads)], 1.0 / SC, None,
                                ALU.mult).then_inc(bias_done, 1)

            def extra(n, s, half):
                m = n + 1
                here = not isinstance(n, int) or n < B - 1
                before = not isinstance(n, int) or n > 0
                to = 1 - half
                if s == 0 and here:
                    dve.wait_ge(chi_done, m + 1)
                    V.scalar_tensor_tensor(clo, bank[BANK_X[1]][:, 0:S], XS / XW, chi, ALU.mult, ALU.subtract)\
                     .then_inc(clo_done, 1)
                if s == 1 and here:
                    dve.wait_ge(qhi_done, m + 1)
                    qv = qs.rearrange("p t h d -> p (t h) d")
                    V.scalar_tensor_tensor(qv[:, :, HD:2 * HD], bank[BANK_X[0]][:, :].rearrange("p (h d) -> p h d", d=HD),
                                           QS / XW, qv[:, :, 0:HD], ALU.mult, ALU.subtract).then_inc(qlo_done, 1)
                if s in (3, 4) and here:
                    t = s - 3
                    x_ = bank[BANK_X[1 - t]]
                    dve.wait_ge(kvhi_done, m * QT + t + 1)
                    V.scalar_tensor_tensor(ks[:, t, :, 2 * HD:3 * HD], x_[:, 0:H].rearrange("p (h d) -> p h d", d=HD),
                                           QS / XW, ks[:, t, :, 0:HD], ALU.mult, ALU.subtract)
                    v = vs[:, to * QT + t]
                    V.scalar_tensor_tensor(v[:, :, HD + 2:2 * HD + 2], x_[:, H:2 * H].rearrange("p (h d) -> p h d", d=HD),
                                           XS / XW, v[:, :, 0:HD], ALU.mult, ALU.subtract).then_inc(kvlo_done, 1)
                if s in (6, 10) and here:
                    t = (s - 6) // 4
                    dve.wait_ge(kT_ps, m * QT + t + 1)
                    V.tensor_copy(kT[:, :, to * S + t * P:to * S + (t + 1) * P],
                                  bank16[BANK_X[0]].rearrange("p (c q) -> p c q", c=8)).then_inc(kT_done, 1)
                if s == 5 and before:
                    dve.wait_ge(ohi_done, n)
                    V.scalar_tensor_tensor(olo.rearrange("p c q -> p (c q)"), bank[BANK_X[1]][:, :], 1.0,
                                           ohi.rearrange("p c q -> p (c q)"), ALU.mult, ALU.subtract).then_inc(olo_done, 1)
                if s == 8 and before:
                    dve.wait_ge(xres_in, n * 16)
                    dve.wait_ge(bs_done, n * 16)
                    dve.wait_ge(wo_ps, n)
                    V.scalar_tensor_tensor(base.rearrange("p t h -> p (t h)"), bank[BANK_X[0]][:, :], 1.0 / XW,
                                           xres.rearrange("p t h -> p (t h)"), ALU.mult, ALU.add).then_inc(base_done, 1)

            def step(n, s, half, extra):
                if lagged(n, s, 0) is not None:
                    row_max(n, s)
                if s in (7, 11):
                    extra(n, s - 1, half)
                if lagged(n, s, 0) is not None:
                    bias(n, s)
                if lagged(n, s, LAG_LO) is not None:
                    dve.wait_ge(pthi_done, n * UNITS + s - LAG_LO + 1)
                    V.scalar_tensor_tensor(ptlo[:, (s - LAG_LO) % 4], bank[BANK_T[(s - LAG_LO) % 2]][:, :], PS,
                                           pthi[:, (s - LAG_LO) % 4], ALU.mult, ALU.subtract).then_inc(ptlo_done, 1)
                v = lagged(n, s, LAG_V)
                if v == 3:
                    tile_out(n, 0, half)
                if v == 11:
                    tile_out(n - 1, 1, 1 - half)
                if s and s not in (7, 11):
                    extra(n, s - 1, half)

            V.tensor_tensor(ge[0:1], jr[0:1, :].rearrange("p (j a) -> p j a", a=1).broadcast_to([1, SLOT_TILES, E]),
                            firsts[0:1].rearrange("p (a e) -> p a e", a=1).broadcast_to([1, SLOT_TILES, E]),
                            ALU.is_ge).then_inc(te_step, 1)
            attention(dve, step, extra, LAG_V)

            def rows_lo(n, u):
                dve.wait_ge(xgh_done, n + 1)
                V.scalar_tensor_tensor(xgl[:, u % 2], bank[u % 2][:, 0:2 * P], XS, xgh[:, u % 2], ALU.mult,
                                       ALU.subtract).then_inc(xgl_done, 1)

            def inner(n, u):
                dve.wait_ge(sg_done, n + 1)
                V.scalar_tensor_tensor(hx[:, u % 2, 0:I], bank[2 + u % 2][:, I:2 * I], XS / XW, sg[:, u % 2],
                                       ALU.mult, ALU.mult)
                V.scalar_tensor_tensor(hx[:, u % 2, P + HALF:I + HALF], bank[2 + u % 2][:, I + P:2 * I], XS / XW,
                                       sg[:, u % 2, P:I], ALU.mult, ALU.mult).then_inc(h_done, 1)

            def inner_lo(n, u):
                dve.wait_ge(hth_done, n + 1)
                V.scalar_tensor_tensor(htl[:, u % 2], bank[4 + u % 2][:, 0:2 * P], 1.0, hth[:, u % 2], ALU.mult,
                                       ALU.subtract).then_inc(htl_done, 1)

            def rows_out(n, u, rounds):
                if u % 2 == 0:
                    return
                dve.wait_ge(y_ps, n + 1)
                dve.wait_ge(ys_done[u], rounds * 16 + 16)
                V.tensor_scalar(yb[:, u], bank[7][:, 0:H], 1.0 / XW, None, ALU.mult).then_inc(y_done[1], 1)

            expert_rounds(dve, (rows_lo, inner, inner_lo, rows_out))


            def shared_inner(g, f):
                dve.wait_ge(silu_done, g * NF + f + 1)
                dve.wait_ge(u_ps, g * NF + f + 1)
                V.scalar_tensor_tensor(hf[:, f % 2], bank[2 * (f % 2) + 1][:, :], XS / XW, sgs[:, f % 2],
                                       ALU.mult, ALU.mult).then_inc(f_done, 1)
                dve.wait_ge(fhi_done, g * NF + f + 1)
                V.tensor_tensor(hlo[:, f % 2], hf[:, f % 2], hhi[:, f % 2], ALU.subtract).then_inc(flo_done, 1)

            def shared_out(g):
                dve.wait_ge(base_in, g * 16 + 16)
                dve.wait_ge(d_ps, g * NF + NF)
                for t in range(TT):
                    V.scalar_tensor_tensor(acc[:, t, 0], bank[4 + t // 2][:, (t % 2) * H:(t % 2 + 1) * H],
                                           sgate[:, bass.ds(g * TT + t, 1)], baser[:, t], ALU.mult,
                                           ALU.add).then_inc(d_used, 1)

            def expert_sum(g, t):
                tk = g * TT + t
                if t == 0:
                    dve.wait_ge(out_done, g * 16 + 16)
                dve.wait_ge(yg_in[t], g * 64 + 64)
                dve.wait_ge(d_used, tk + 5)
                for k in range(TOPK):
                    if k:
                        dve.wait_ge(acc_done, (TOPK - 1) * tk + k)
                    dst = yout[:, t] if k == TOPK - 1 else acc[:, t, (k + 1) % 2]
                    ins = V.scalar_tensor_tensor(dst, yg[:, t, k], cw4[:, bass.ds(tk, 1), k].rearrange("p a -> p a"),
                                                 acc[:, t, k % 2], ALU.mult, ALU.add)
                    ins.then_inc(tok_done if k == TOPK - 1 else acc_done, 1)

            for f in range(NF):
                shared_inner(0, f)
            with dve.Fori(1, NG) as g:
                shared_out(g - 1)
                for f in range(NF):
                    shared_inner(g, f)
                    if f < TT:
                        expert_sum(g - 1, f)
            shared_out(NG - 1)
            for t in range(TT):
                expert_sum(NG - 1, t)

        @block.tensor
        def _(pe):
            mm = nc.tensor.matmul

            def three(dst, pairs, start=True, stop=True, **more):
                n = 0
                for (lh, ll), (rh, rl) in pairs:
                    for a, b in ((lh, rh), (lh, rl), (ll, rh)):
                        last = mm(dst, a, b, start=start and n == 0, stop=stop and n == 3 * len(pairs) - 1, **more)
                        n += 1
                return last

            pe.wait_ge(prep, 1)
            pe.wait_ge(small_done, 2)

            with pe.Fori(0, NG) as g:
                pe.wait_ge(xn_done, g * TT + TT)
                for c in range(KC):
                    for t in range(TT):
                        last = nc.tensor.transpose(bank[c][:, t * P:(t + 1) * P], xn[:, t, c * P:(c + 1) * P], idf[:, :])
                    last.then_inc(xt_ps, 1)
                pe.wait_ge(xhi_done, g * KC + KC)
                pe.wait_ge(xlo_done, g * KC + KC)
                for t in range(TT):
                    ts = bass.ds(g * GT + t * P, P)
                    last = three(bank[2][:, t * RPAD:t * RPAD + NR],
                                 [((xhi[:, k, ts], xlo[:, k, ts]), [w[:, 0:NR] for w in cols(W_R, k, RPAD)]) for k in range(KC)])
                last.then_inc(rt_ps, 1)

            pe.wait_ge(pre_done, 1)
            mm(bank[0][:, :], onesh[:, :], pre[:, PRE, 0:TILES * E], start=True, stop=False)
            mm(bank[0][:, :], trih[:, :], msk.rearrange("p t e -> p (t e)"), start=False, stop=True)
            mm(bank[1][:, 0:E], onesh[:, :], pre[:, PRE, TILES * E:], start=True, stop=True).then_inc(pos_ps, 1)
            pe.wait_ge(aux_done, 1)

            def scores(n, u, half):
                qt, heads, nk = unit(u)
                dst = bank[BANK_S[u % 3]][:, :].rearrange("p (h k) -> p h k", k=nk * P)
                if u == 0:
                    pe.wait_ge(qT_done, n * QT + QT)
                    pe.wait_ge(kT_done, n * QT + QT)
                if not isinstance(n, int) or n * UNITS + u >= 3:
                    pe.wait_ge(exp_done, n * UNITS + u - 2)
                b0 = half * S
                for j, h in enumerate(heads):
                    r = 64 * (h % 2)
                    last = mm(dst[:, j], qT[r:r + 64, h // 2, b0 + qt * P:b0 + (qt + 1) * P],
                              kT[r:r + 64, h // 2, b0:b0 + nk * P],
                              start=j == 0, stop=False, skip_group_check=True)
                last = mm(dst[:, :, (nk - 1) * P:nk * P], idb[:, :],
                          maskb[:, :].rearrange("p (a k) -> p a k", a=1).broadcast_to([P, len(heads), P]),
                          start=False, stop=True, skip_group_check=True)
                last.then_inc(s_ps, 1)

            def transpose_probs(n, s):
                m = s - LAG_T
                pe.wait_ge(exp_done, n * UNITS + m + 1)
                if not isinstance(n, int) or n * UNITS + m >= 2:
                    pe.wait_ge(ptlo_done, n * UNITS + m - 1)
                for i in range(4):
                    last = nc.tensor.transpose(bank[BANK_T[m % 2]][:, i * P:(i + 1) * P], prob[:, m % 3, i], idf[:, :])
                last.then_inc(pt_ps, 1)

            def values(n, s, u, half):
                qt, heads, nk = unit(u)
                pe.wait_ge(ptlo_done, n * UNITS + s - LAG_V + 1)
                if u in (0, 4):
                    pe.wait_ge(o_used, n * QT + qt + 1)
                o = bank[BANK_O][:, :].rearrange("p (h c) -> p h c", h=HEADS)
                for j, h in enumerate(heads):
                    for k in range(nk):
                        v = vs[:, half * QT + k, h]
                        hi, lo = (w[:, u % 4, (j * nk + k) * P:(j * nk + k + 1) * P] for w in (pthi, ptlo))
                        mm(o[:, h, 0:HD + 1], hi, v[:, 0:HD + 1], start=k == 0, stop=False, skip_group_check=True)
                        mm(o[:, h, 0:HD], hi, v[:, HD + 2:2 * HD + 2], start=False, stop=False, skip_group_check=True)
                        last = mm(o[:, h, 0:HD + 1], lo, v[:, 0:HD + 1], start=False, stop=k == nk - 1,
                                  skip_group_check=True)
                last.then_inc(pv_ps, 1)

            def extra(n, s, half):
                m = n + 1
                here = not isinstance(n, int) or n < B - 1
                before = not isinstance(n, int) or n > 0
                if s == 0 and here:
                    ts = bass.ds(m * S, S)
                    three(bank[BANK_X[1]][:, 0:S],
                          [(cols(W_DKV, k, KV), (xhi[:, k, ts], xlo[:, k, ts])) for k in range(KC)]).then_inc(c_ps, 1)
                if s == 1 and here:
                    for t in range(QT):
                        ts = bass.ds(m * S + t * P, P)
                        last = three(bank[BANK_X[0]][:, t * H:(t + 1) * H],
                                     [((xhi[:, k, ts], xlo[:, k, ts]), cols(W_Q, k, H)) for k in range(KC)])
                    last.then_inc(q_ps, 1)
                if s in (3, 4) and here:
                    t = s - 3
                    pe.wait_ge(clo_done, m + 1)
                    if t:
                        pe.wait_ge(qlo_done, m + 1)
                    ts = slice(t * P, (t + 1) * P)
                    three(bank[BANK_X[1 - t]][:, :], [((chi[:, ts], clo[:, ts]), cols(W_UKV, 0, 2 * H))]).then_inc(kv_ps, 1)
                if s in (7, 9) and here:
                    t = (s - 7) // 2
                    if t:
                        pe.wait_ge(qT_done, m * QT + 1)
                    elif before:
                        pe.wait_ge(olo_done, n)
                    for c in range(8):
                        last = nc.tensor.transpose(bank16[BANK_X[1]][:, c * P:(c + 1) * P],
                                                   qs[:, t, 2 * c:2 * c + 2].rearrange("p h d -> p (h d)"), idh[:, :])
                    last.then_inc(qT_ps, 1)
                if s in (6, 10) and here:
                    t = (s - 6) // 4
                    if not t:
                        pe.wait_ge(kvlo_done, m * QT + 2)
                    elif before:
                        pe.wait_ge(base_done, n)
                    else:
                        pe.wait_ge(kT_done, m * QT + 1)
                    for c in range(8):
                        last = nc.tensor.transpose(bank16[BANK_X[0]][:, c * P:(c + 1) * P],
                                                   ks[:, t, 2 * c:2 * c + 2].rearrange("p h d -> p (h d)"), idh[:, :])
                    last.then_inc(kT_ps, 1)
                if s == 5 and before:
                    pe.wait_ge(o_used, n * QT + 1)
                    if here:
                        pe.wait_ge(kvlo_done, m * QT + 1)
                    for c in range(KC):
                        for t in range(QT):
                            last = nc.tensor.transpose(bank[BANK_X[1]][:, (c * QT + t) * P:(c * QT + t + 1) * P],
                                                       onat[:, 1 - half, t, c * P:(c + 1) * P], idf[:, :])
                    last.then_inc(oT_ps, 1)
                if s == 8 and before:
                    pe.wait_ge(olo_done, n)
                    if here:
                        pe.wait_ge(kT_done, m * QT + 1)
                    for t in range(QT):
                        ts = slice(t * P, (t + 1) * P)
                        last = three(bank[BANK_X[0]][:, t * H:(t + 1) * H],
                                     [((ohi[:, k, ts], olo[:, k, ts]), cols(W_O, k, H)) for k in range(KC)])
                    last.then_inc(wo_ps, 1)

            def step(n, s, half, extra):
                if lagged(n, s, 0) is not None:
                    scores(n, s, half)
                if lagged(n, s, LAG_T) is not None:
                    transpose_probs(n, s)
                v = lagged(n, s, LAG_V)
                if v is not None:
                    values(n, s, v, half if s >= LAG_V else 1 - half)
                extra(n, s, half)

            attention(pe, step, extra, LAG_V)

            pe.wait_ge(wlo_done, 2 + E + len(SHARED))
            pe.wait_ge(base_done, B)

            pe.wait_ge(pair_done, E)
            pe.wait_ge(te_step, E.bit_length() + 1)
            offs = [pe.alloc_register(f"expert_columns{u}") for u in range(U)]

            def expert(n, u):
                pe.reg_load(offs[u], texp[0:1, bass.ds(n, 1)])

            def columns_of(u):
                return pe.snap(offs[u], min_val=0, max_val=(E - 1) * EW)

            def rows(n, u, rounds):
                pe.wait_ge(xg_in[u], rounds * 16 + 16)
                pe.wait_ge(xgl_done, n + 1)
                for c in range(KC):
                    last = nc.tensor.transpose(bank[u % 2][:, c * P:(c + 1) * P], xg[:, u, c * P:(c + 1) * P], idf[:, :])
                last.then_inc(tx_ps, 1)

            def gate_up(n, u):
                off = columns_of(u)
                pe.wait_ge(xgl_done, n + 3)
                pe.wait_ge(h_done, n + 1)
                three(bank[2 + u % 2][:, 0:GU],
                      [((xgh[:, u % 2, c * P:(c + 1) * P], xgl[:, u % 2, c * P:(c + 1) * P]),
                        [w[:, bass.ds(off + c * GU, GU)] for w in (whi, wlo)]) for c in range(KC)]).then_inc(gu_ps, 1)

            def turn(n, u):
                pe.wait_ge(h_done, n + 3)
                pe.wait_ge(htl_done, n + 1)
                for c in range(2):
                    last = nc.tensor.transpose(bank[4 + u % 2][:, c * P:(c + 1) * P], hx[:, u % 2, c * P:(c + 1) * P], idf[:, :])
                last.then_inc(th_ps, 1)

            def down(n, u, rounds):
                off = columns_of(u)
                pe.wait_ge(htl_done, n + 3)
                pe.wait_ge(y_done[u % 2], rounds * 2 + u // 2 + 1)
                y = bank[6 + u % 2][:, 0:H]
                three(y, [((hth[:, u % 2, 0:P], htl[:, u % 2, 0:P]),
                           [w[:, bass.ds(off + KC * GU, H)] for w in (whi, wlo)])], stop=False)
                c = off + KC * GU + H
                mm(y, hth[:, u % 2, P:2 * P], whi[:, bass.ds(c, H)], start=False, stop=False)
                mm(y, htl[0:I - P, u % 2, P:2 * P], whi[0:I - P, bass.ds(c, H)], start=False, stop=True).then_inc(y_ps, 1)

            last_round = SLOT_TILES // U

            def take(i, u):
                for k, stepk in enumerate((rows, gate_up, turn, down)):
                    n = i * U + u - k
                    if k == 2 and not (isinstance(i, int) and i * U + u >= SLOT_TILES):
                        expert(i * U + u, u)
                    if isinstance(i, int) and not 0 <= n < SLOT_TILES:
                        continue
                    r = i if u >= k else i - 1
                    if k in (0, 3):
                        stepk(n, (u - k) % U, r)
                    else:
                        stepk(n, (u - k) % U)

            for u in range(U):
                take(0, u)
            with pe.Fori(1, last_round) as i:
                for u in range(U):
                    take(i, u)
            for u in range(3):
                take(last_round, u)

            with pe.Fori(0, NG) as g:
                gs = bass.ds(g * GT, GT)
                for f in range(NF + 1):
                    if f < NF:
                        n = g * NF + f
                        off = W_F + f * FW
                        pe.wait_ge(f_done, n + 1)
                        three(bank[2 * (f % 2)][:, :], [(cols(off, k, P), (xhi[:, k, gs], xlo[:, k, gs])) for k in range(KC)])\
                            .then_inc(g_ps, 1)
                        three(bank[2 * (f % 2) + 1][:, :],
                              [(cols(off, KC + k, P), (xhi[:, k, gs], xlo[:, k, gs])) for k in range(KC)]).then_inc(u_ps, 1)
                    if f:
                        pe.wait_ge(flo_done, g * NF + f)
                        if f == 1:
                            pe.wait_ge(d_used, g * TT + 4)
                        o = W_F + (f - 1) * FW + 2 * KC * P
                        for t in range(TT):
                            ts = slice(t * P, (t + 1) * P)
                            last = three(bank[4 + t // 2][:, (t % 2) * H:(t % 2 + 1) * H],
                                         [((hhi[:, (f - 1) % 2, ts], hlo[:, (f - 1) % 2, ts]), (whi[:, o:o + H], wlo[:, o:o + H]))],
                                         start=f == 1 and t % 2 == 0, stop=f == NF, skip_group_check=True)
                        last.then_inc(d_ps, 1)


def weight_columns(w_dkv, w_q, w_uk, w_uv, w_o, gate_w, gate_up, down, shared_gate_up, shared_down, shared_vec):
    f32 = np.float32
    pad = np.zeros((NF * P - SI, H), f32)
    out = np.zeros((P, W_ALL), f32)
    for e in range(E):
        dst = out[:, e * EW:(e + 1) * EW]
        dst[:, :KC * GU] = gate_up[e].T.reshape(KC, P, GU).transpose(1, 0, 2).reshape(P, KC * GU)
        dst[:, KC * GU:KC * GU + H] = down[e].T[:P]
        dst[:I - P, KC * GU + H:] = down[e].T[P:]
        dst[HALF:HALF + I - P, KC * GU + H:] = down[e].T[P:]
    gate = np.concatenate([shared_gate_up[:SI], pad])
    up = np.concatenate([shared_gate_up[SI:], pad])
    dn = np.concatenate([shared_down.T, pad])
    gu = np.stack([gate.reshape(NF, P, KC, P), up.reshape(NF, P, KC, P)], 1).transpose(4, 0, 1, 3, 2).reshape(P, NF, 2 * KC * P)
    out[:, W_F:W_Q] = np.concatenate([gu, dn.reshape(NF, P, H).transpose(1, 0, 2)], 2).reshape(P, W_Q - W_F)

    def chunked(w, n):
        return w.T.reshape(-1, P, n).transpose(1, 0, 2).reshape(P, -1)

    out[:, W_Q:W_DKV] = chunked(w_q, H)
    out[:, W_DKV:W_UKV] = chunked(w_dkv, KV)
    out[:, W_UKV:W_O] = np.concatenate([w_uk.T, w_uv.T], 1)
    out[:, W_O:W_R] = chunked(w_o, H)
    r = np.zeros((RPAD, H), f32)
    r[:E], r[E:NR] = gate_w, shared_vec
    out[:, W_R:] = chunked(r, RPAD)
    return out


def constants():
    f32 = np.float32
    p = np.arange(P)
    ident = np.eye(P, dtype=f32)
    mask = np.where(p[None, :] > p[:, None], NEG, 0).astype(f32)
    auxq, auxk = np.zeros((P, 2, 16), f32), np.zeros((P, 2, 16), f32)
    pos = p[:, None] + P * np.arange(2)[None, :]
    auxq[:, :, 0], auxq[:, :, 1] = 1, -SC * SLOPE * pos
    auxk[:, :, 0], auxk[:, :, 1] = SC * SLOPE * pos, 1
    iota = np.tile(np.arange(E, dtype=f32), (P, 1))
    tri = (p[:, None] < p[None, :]).astype(f32)
    tids = (p[:, None] + P * np.arange(TILES)[None, :]).astype(np.int32)
    jrow = np.arange(SLOT_TILES, dtype=f32)[None, :]
    return ident, mask, auxq, auxk, iota, tri, tids, jrow


def kernel(**inputs):
    import concourse.bacc as _bacc
    from concourse.bass_utils import run_bass_kernel_spmd as _run

    a = {k: np.asarray(v) for k, v in inputs.items()}
    wall = weight_columns(*(a[k] for k in (
        "L0_attn_w_dkv", "L0_attn_w_q", "L0_attn_w_uk", "L0_attn_w_uv", "L0_attn_w_o", "L0_ffn_gate_w",
        "L0_ffn_expert_gate_up", "L0_ffn_expert_down", "L0_ffn_shared_gate_up", "L0_ffn_shared_down",
        "L0_ffn_shared_gate_vec")))
    ident, mask, auxq, auxk, iota, tri, tids, jrow = constants()
    arrays = {"x": np.ascontiguousarray(a["L0_attn_hidden_states"].reshape(TOK, H)), "wall": wall, "ident": ident,
              "mask": mask, "auxq": auxq, "auxk": auxk, "iota": iota, "tri": tri,
              "tids": tids, "jrow": jrow}
    nc = _bacc.Bacc("TRN2", target_bir_lowering=False, num_devices=1)
    args = [nc.dram_tensor(f"in_{n}", v.shape, mybir.dt.from_np(v.dtype), kind="ExternalInput").ap()
            for n, v in arrays.items()]
    out = nc.dram_tensor("out", (TOK, H), F32, kind="ExternalOutput").ap()
    build(nc, *args, out)
    r = _run(nc, [{f"in_{n}": v for n, v in arrays.items()}], core_ids=[0])
    return r.results[0]["out"].reshape(B, S, H)
```
